# Optimizing a Trainium2 kernel written in Bass

```python
import numpy as np
import jax
import jax.numpy as jnp

def _softmax(x, axis=-1):
    return jax.nn.softmax(x, axis=axis)

def _gelu(x):
    return jax.nn.gelu(x, approximate=True)

def _silu(x):
    return jax.nn.silu(x)

def _sigmoid(x):
    return jax.nn.sigmoid(x)

def _layernorm(x, axis=-1, eps=1e-05):
    m = jnp.mean(x, axis=axis, keepdims=True)
    v = jnp.var(x, axis=axis, keepdims=True)
    return (x - m) / jnp.sqrt(v + eps)

def _scatter_add(tgt, idx, src, axis=0):
    return tgt.at[idx].add(src)

def _segment_sum(src, seg, n):
    return jax.ops.segment_sum(src, seg, n)
kernel_name = 'mk_dlrm_tower_d1_rec_r8_1a91f6'

def setup_inputs(seed: int=0):
    np.random.seed(seed)
    _w = jnp.asarray

    def _rec_inputs():
        import jax
        import jax.numpy as jnp
        _tk = jax.random.key(seed)
        dense_ctx = jax.random.normal(jax.random.fold_in(_tk, 190), (2048, 16), jnp.float32)
        ids = jnp.stack([jax.random.randint(jax.random.fold_in(_tk, 200 + f), (2048,), 0, v, jnp.int32) for f, v in enumerate([1000, 12500, 1250, 12500, 1000, 1000, 1000, 1000, 12500, 1250, 1000, 1250, 1000, 1250, 1250, 12500, 1250, 12500, 1250, 1250, 12500, 1000, 12500, 12500, 1250, 1000, 1250, 1250, 1250, 1000, 1000, 1000])], axis=1)
        tbl_0 = 0.05 * jax.random.normal(jax.random.fold_in(_tk, 500 + 0), (1000, 256), jnp.float32)
        tbl_1 = 0.05 * jax.random.normal(jax.random.fold_in(_tk, 500 + 1), (12500, 256), jnp.float32)
        tbl_2 = 0.05 * jax.random.normal(jax.random.fold_in(_tk, 500 + 2), (1250, 256), jnp.float32)
        tbl_3 = 0.05 * jax.random.normal(jax.random.fold_in(_tk, 500 + 3), (12500, 256), jnp.float32)
        tbl_4 = 0.05 * jax.random.normal(jax.random.fold_in(_tk, 500 + 4), (1000, 256), jnp.float32)
        tbl_5 = 0.05 * jax.random.normal(jax.random.fold_in(_tk, 500 + 5), (1000, 256), jnp.float32)
        tbl_6 = 0.05 * jax.random.normal(jax.random.fold_in(_tk, 500 + 6), (1000, 256), jnp.float32)
        tbl_7 = 0.05 * jax.random.normal(jax.random.fold_in(_tk, 500 + 7), (1000, 256), jnp.float32)
        tbl_8 = 0.05 * jax.random.normal(jax.random.fold_in(_tk, 500 + 8), (12500, 256), jnp.float32)
        tbl_9 = 0.05 * jax.random.normal(jax.random.fold_in(_tk, 500 + 9), (1250, 256), jnp.float32)
        tbl_10 = 0.05 * jax.random.normal(jax.random.fold_in(_tk, 500 + 10), (1000, 256), jnp.float32)
        tbl_11 = 0.05 * jax.random.normal(jax.random.fold_in(_tk, 500 + 11), (1250, 256), jnp.float32)
        tbl_12 = 0.05 * jax.random.normal(jax.random.fold_in(_tk, 500 + 12), (1000, 256), jnp.float32)
        tbl_13 = 0.05 * jax.random.normal(jax.random.fold_in(_tk, 500 + 13), (1250, 256), jnp.float32)
        tbl_14 = 0.05 * jax.random.normal(jax.random.fold_in(_tk, 500 + 14), (1250, 256), jnp.float32)
        tbl_15 = 0.05 * jax.random.normal(jax.random.fold_in(_tk, 500 + 15), (12500, 256), jnp.float32)
        tbl_16 = 0.05 * jax.random.normal(jax.random.fold_in(_tk, 500 + 16), (1250, 256), jnp.float32)
        tbl_17 = 0.05 * jax.random.normal(jax.random.fold_in(_tk, 500 + 17), (12500, 256), jnp.float32)
        tbl_18 = 0.05 * jax.random.normal(jax.random.fold_in(_tk, 500 + 18), (1250, 256), jnp.float32)
        tbl_19 = 0.05 * jax.random.normal(jax.random.fold_in(_tk, 500 + 19), (1250, 256), jnp.float32)
        tbl_20 = 0.05 * jax.random.normal(jax.random.fold_in(_tk, 500 + 20), (12500, 256), jnp.float32)
        tbl_21 = 0.05 * jax.random.normal(jax.random.fold_in(_tk, 500 + 21), (1000, 256), jnp.float32)
        tbl_22 = 0.05 * jax.random.normal(jax.random.fold_in(_tk, 500 + 22), (12500, 256), jnp.float32)
        tbl_23 = 0.05 * jax.random.normal(jax.random.fold_in(_tk, 500 + 23), (12500, 256), jnp.float32)
        tbl_24 = 0.05 * jax.random.normal(jax.random.fold_in(_tk, 500 + 24), (1250, 256), jnp.float32)
        tbl_25 = 0.05 * jax.random.normal(jax.random.fold_in(_tk, 500 + 25), (1000, 256), jnp.float32)
        tbl_26 = 0.05 * jax.random.normal(jax.random.fold_in(_tk, 500 + 26), (1250, 256), jnp.float32)
        tbl_27 = 0.05 * jax.random.normal(jax.random.fold_in(_tk, 500 + 27), (1250, 256), jnp.float32)
        tbl_28 = 0.05 * jax.random.normal(jax.random.fold_in(_tk, 500 + 28), (1250, 256), jnp.float32)
        tbl_29 = 0.05 * jax.random.normal(jax.random.fold_in(_tk, 500 + 29), (1000, 256), jnp.float32)
        tbl_30 = 0.05 * jax.random.normal(jax.random.fold_in(_tk, 500 + 30), (1000, 256), jnp.float32)
        tbl_31 = 0.05 * jax.random.normal(jax.random.fold_in(_tk, 500 + 31), (1000, 256), jnp.float32)
        _rk = jax.random.fold_in(_tk, 7)
        W_top1 = 0.0441942 * jax.random.normal(jax.random.fold_in(_tk, 801), (512, 512), jnp.float32)
        W_top2 = 0.0441942 * jax.random.normal(jax.random.fold_in(_tk, 802), (512, 256), jnp.float32)
        W_top3 = 0.0625 * jax.random.normal(jax.random.fold_in(_tk, 803), (256, 1), jnp.float32)
        b_top1 = jnp.zeros((512,), jnp.float32)
        b_top2 = jnp.zeros((256,), jnp.float32)
        return (dense_ctx, ids, tbl_0, tbl_1, tbl_2, tbl_3, tbl_4, tbl_5, tbl_6, tbl_7, tbl_8, tbl_9, tbl_10, tbl_11, tbl_12, tbl_13, tbl_14, tbl_15, tbl_16, tbl_17, tbl_18, tbl_19, tbl_20, tbl_21, tbl_22, tbl_23, tbl_24, tbl_25, tbl_26, tbl_27, tbl_28, tbl_29, tbl_30, tbl_31, W_top1, b_top1, W_top2, b_top2, W_top3)
    dense_ctx, ids, tbl_0, tbl_1, tbl_2, tbl_3, tbl_4, tbl_5, tbl_6, tbl_7, tbl_8, tbl_9, tbl_10, tbl_11, tbl_12, tbl_13, tbl_14, tbl_15, tbl_16, tbl_17, tbl_18, tbl_19, tbl_20, tbl_21, tbl_22, tbl_23, tbl_24, tbl_25, tbl_26, tbl_27, tbl_28, tbl_29, tbl_30, tbl_31, W_top1, b_top1, W_top2, b_top2, W_top3 = _rec_inputs()

    def _L0_rec_setup():
        import jax, jax.numpy as jnp
        import numpy as np
        B, N, D = (1024, 32, 256)
        key = jax.random.key(seed)
        x = jax.random.normal(key, (B, N, D), dtype=jnp.float32)
        return {'x': x}
    _L0_rec_all = _L0_rec_setup()
    _L0_rec_in = {k: v for k, v in _L0_rec_all.items() if k in ()}
    del _L0_rec_all
    return {'dense_ctx': dense_ctx, 'ids': ids, 'tbl_0': tbl_0, 'tbl_1': tbl_1, 'tbl_2': tbl_2, 'tbl_3': tbl_3, 'tbl_4': tbl_4, 'tbl_5': tbl_5, 'tbl_6': tbl_6, 'tbl_7': tbl_7, 'tbl_8': tbl_8, 'tbl_9': tbl_9, 'tbl_10': tbl_10, 'tbl_11': tbl_11, 'tbl_12': tbl_12, 'tbl_13': tbl_13, 'tbl_14': tbl_14, 'tbl_15': tbl_15, 'tbl_16': tbl_16, 'tbl_17': tbl_17, 'tbl_18': tbl_18, 'tbl_19': tbl_19, 'tbl_20': tbl_20, 'tbl_21': tbl_21, 'tbl_22': tbl_22, 'tbl_23': tbl_23, 'tbl_24': tbl_24, 'tbl_25': tbl_25, 'tbl_26': tbl_26, 'tbl_27': tbl_27, 'tbl_28': tbl_28, 'tbl_29': tbl_29, 'tbl_30': tbl_30, 'tbl_31': tbl_31, 'W_top1': W_top1, 'b_top1': b_top1, 'W_top2': W_top2, 'b_top2': b_top2, 'W_top3': W_top3}

def reference(dense_ctx, ids, tbl_0, tbl_1, tbl_2, tbl_3, tbl_4, tbl_5, tbl_6, tbl_7, tbl_8, tbl_9, tbl_10, tbl_11, tbl_12, tbl_13, tbl_14, tbl_15, tbl_16, tbl_17, tbl_18, tbl_19, tbl_20, tbl_21, tbl_22, tbl_23, tbl_24, tbl_25, tbl_26, tbl_27, tbl_28, tbl_29, tbl_30, tbl_31, W_top1, b_top1, W_top2, b_top2, W_top3):
    import jax
    import jax.numpy as jnp

    def _L0_rec_ref(x):
        import jax, jax.numpy as jnp
        import numpy as np
        B, N, D = (1024, 32, 256)
        'Second-order feature interaction (DLRM dot interaction).\n\n            Computes dot(x_i, x_j) for all field pairs i < j (self_interaction=False),\n            flattened in row-major upper-triangular order -> [B, N*(N-1)/2].\n            Matches tf.boolean_mask(dot_products, strictly_upper_mask) ordering.\n            '
        b, n, d = x.shape
        iu, ju = jnp.triu_indices(n, k=1)
        dots = jnp.einsum('bnd,bmd->bnm', x, x)
        return dots[:, iu, ju]
    e = jnp.stack([tbl_0[ids[:, 0]], tbl_1[ids[:, 1]], tbl_2[ids[:, 2]], tbl_3[ids[:, 3]], tbl_4[ids[:, 4]], tbl_5[ids[:, 5]], tbl_6[ids[:, 6]], tbl_7[ids[:, 7]], tbl_8[ids[:, 8]], tbl_9[ids[:, 9]], tbl_10[ids[:, 10]], tbl_11[ids[:, 11]], tbl_12[ids[:, 12]], tbl_13[ids[:, 13]], tbl_14[ids[:, 14]], tbl_15[ids[:, 15]], tbl_16[ids[:, 16]], tbl_17[ids[:, 17]], tbl_18[ids[:, 18]], tbl_19[ids[:, 19]], tbl_20[ids[:, 20]], tbl_21[ids[:, 21]], tbl_22[ids[:, 22]], tbl_23[ids[:, 23]], tbl_24[ids[:, 24]], tbl_25[ids[:, 25]], tbl_26[ids[:, 26]], tbl_27[ids[:, 27]], tbl_28[ids[:, 28]], tbl_29[ids[:, 29]], tbl_30[ids[:, 30]], tbl_31[ids[:, 31]]], axis=1)
    z = _L0_rec_ref(e)
    z = z.reshape(z.shape[0], -1)
    h = jnp.concatenate([z, dense_ctx], axis=1)
    h = jnp.maximum(h @ W_top1 + b_top1, 0.0)
    h = jnp.maximum(h @ W_top2 + b_top2, 0.0)
    y = h @ W_top3
    return y

_drawn_inputs = setup_inputs


def setup_inputs(seed=0):
    import zlib

    import numpy as np

    out = dict(_drawn_inputs(seed))
    spreads = {'b_top1': (0.0, 0.1), 'b_top2': (0.0, 0.1)}
    factors = {}
    for name, (base, spread) in spreads.items():
        noise = np.random.default_rng([zlib.crc32(name.encode()), seed]).standard_normal(out[name].shape)
        drawn = base * np.exp(spread * noise) if base else spread * noise
        out[name] = jnp.asarray(drawn.astype(out[name].dtype))
    for name, factor in factors.items():
        out[name] = (out[name] * factor).astype(out[name].dtype)
    return out
```

```python
from contextlib import ExitStack

import concourse.bass as bass
from concourse import mybir

P = 128
NFIELD = 32
NDIM = 256
NCHUNK = NDIM // P
NDENSE = 16
UNIT = 4
NUNIT = NFIELD // UNIT
NQUAD = 4
NGROUP = P // NQUAD
GPU = 8
NGU = NGROUP // GPU
LEAD = 16
NPAIR = NFIELD * (NFIELD - 1) // 2
SLOTS = 2


def first_pair(i):
    return i * (NFIELD - 1) - i * (i - 1) // 2


def dlrm_tower(nc, dense, ids, tables, w1, b1, w2, b2, w3, eye, out):
    fp32 = mybir.dt.float32
    int32 = mybir.dt.int32
    uint32 = mybir.dt.uint32
    ALU = mybir.AluOpType
    ACT = mybir.ActivationFunctionType

    batch = ids.shape[0]
    ntile = batch // P
    nin, nhid1 = w1.shape
    nhid2 = w2.shape[1]
    K1, M1, M2 = nin // P, nhid1 // P, nhid2 // P
    assert nin == NPAIR + NDENSE and ntile % 2 == 0 and ntile >= 4

    ctx = ExitStack()
    with ctx:
        def sb(name, shape, dt=fp32):
            return ctx.enter_context(nc.sbuf_tensor(name, shape, dt))

        def pb(name, shape):
            return ctx.enter_context(nc.psum_tensor(name, shape, fp32))

        def sem(name):
            return ctx.enter_context(nc.semaphore(name))

        ids_sb = [sb(f"ids_sb{s}", [P, NFIELD], int32) for s in range(SLOTS)]
        rows = [sb(f"rows{s}", [P, NFIELD, NDIM]) for s in range(SLOTS)]
        rows_t = [sb(f"rows_t{s}", [P, NCHUNK, NGROUP, NQUAD, NFIELD]) for s in range(SLOTS)]
        prod = sb("prod", [P, NGROUP, NFIELD])
        feat = sb("feat", [P, LEAD + nin])
        feat_t = sb("feat_t", [P, K1, P])
        hid1 = sb("hid1", [P, M1, P])
        hid2 = sb("hid2", [P, M2, P])
        y_row = sb("y_row", [1, P])
        w1_sb = sb("w1_sb", [P, K1, nhid1])
        w2_sb = sb("w2_sb", [P, M1, nhid2])
        w3_sb = sb("w3_sb", [P, M2])
        b1_sb = sb("b1_sb", [P, M1])
        b2_sb = sb("b2_sb", [P, M2])
        ident = sb("ident", [P, P])

        xp = [pb(f"xp{c}", [P, UNIT, P]) for c in range(NCHUNK)]
        gp = [pb(f"gp{k}", [P, GPU, P]) for k in range(2)]
        mp = pb("mp", [P, 4, P])
        lp = pb("lp", [P, M1, P])

        w_loaded = sem("w_loaded")
        ids_loaded = [sem(f"ids_loaded{s}") for s in range(SLOTS)]
        dense_loaded = sem("dense_loaded")
        gathered = [[sem(f"gathered{s}_{u}") for u in range(NUNIT)] for s in range(SLOTS)]
        transposed = [sem(f"transposed{c}") for c in range(NCHUNK)]
        rows_t_ready = [sem(f"rows_t_ready{c}") for c in range(NCHUNK)]
        multiplied = sem("multiplied")
        prod_act = sem("prod_act")
        prod_dve = sem("prod_dve")
        turned = sem("turned")
        feat_ready = sem("feat_ready")
        feat_transposed = sem("feat_transposed")
        feat_t_ready = sem("feat_t_ready")
        layer1_done = sem("layer1_done")
        hid1_ready = sem("hid1_ready")
        layer2_done = sem("layer2_done")
        hid2_ready = sem("hid2_ready")
        layer3_done = sem("layer3_done")
        y_ready = sem("y_ready")
        y_stored = sem("y_stored")
        NWEIGHT = 6

        block = ctx.enter_context(nc.Block())

        @block.sync
        def _(sp):
            def load_ids(at, s):
                sp.dma_start(ids_sb[s][:, :], ids[bass.ds(at, P), :]).then_inc(ids_loaded[s], 16)

            def load_dense(at):
                sp.dma_start(feat[:, LEAD + NPAIR:], dense[bass.ds(at, P), :]).then_inc(dense_loaded, 16)

            def store_y(t, at):
                sp.wait_ge(y_ready, t + 1)
                sp.dma_start(out[bass.ds(at, P), :].rearrange("b o -> o b"),
                             y_row[0:1, :]).then_inc(y_stored, 16)

            load_ids(0, 0)
            load_ids(P, 1)
            sp.dma_start(ident[:, :], eye).then_inc(w_loaded, 16)
            load_dense(0)
            sp.dma_start(w1_sb[:, :, :], w1.rearrange("(k p) n -> p k n", p=P)).then_inc(w_loaded, 16)
            sp.dma_start(w2_sb[:, :, :], w2.rearrange("(k p) n -> p k n", p=P)).then_inc(w_loaded, 16)
            sp.dma_start(w3_sb[:, :], w3.rearrange("(k p) o -> p (k o)", p=P),
                         allow_slow_non_contiguous=True).then_inc(w_loaded, 16)
            sp.dma_start(b1_sb[:, :], b1.rearrange("(k p) -> p k", p=P),
                         allow_slow_non_contiguous=True).then_inc(w_loaded, 16)
            sp.dma_start(b2_sb[:, :], b2.rearrange("(k p) -> p k", p=P),
                         allow_slow_non_contiguous=True).then_inc(w_loaded, 16)

            def step(t, s):
                here, before, store = sp.snap(t * P), sp.snap(t * P - P), sp.snap(t * P - 2 * P)
                sp.wait_ge(transposed[NCHUNK - 1], (t - 1) * NUNIT)
                load_ids(here, s)
                sp.wait_ge(feat_transposed, t - 1)
                load_dense(before)
                store_y(t - 2, store)

            with sp.Fori(0, ntile // 2 - 1) as i:
                step(2 * i + 2, 0)
                step(2 * i + 3, 1)
            sp.wait_ge(feat_transposed, ntile - 1)
            load_dense((ntile - 1) * P)
            store_y(ntile - 2, (ntile - 2) * P)
            store_y(ntile - 1, (ntile - 1) * P)
            sp.wait_ge(y_stored, 16 * ntile)

        @block.gpsimd
        def _(pool):
            def gather(s, k, first=False):
                pool.wait_ge(ids_loaded[s], 16 * (k + 1))
                for u in range(NUNIT):
                    if not first:
                        pool.wait_ge(transposed[NCHUNK - 1], units_used)
                        pool.reg_add(units_used, units_used, 1)
                    for n in range(u * UNIT, (u + 1) * UNIT):
                        pool.indirect_dma_start(
                            out=rows[s][:, n, :], out_offset=None, in_=tables[n][:, :],
                            in_offset=bass.IndirectOffsetOnAxis(ap=ids_sb[s][:, n:n + 1].bitcast(uint32), axis=0),
                        ).then_inc(gathered[s][u], 16)

            gather(0, 0, first=True)
            gather(1, 0, first=True)
            units_used = pool.alloc_register("units_used")
            pool.reg_mov(units_used, 1)
            with pool.Fori(1, ntile // 2) as k:
                gather(0, k)
                gather(1, k)

        @block.tensor
        def _(pe):
            def transpose_unit(t, s, k, u, first=False):
                pe.wait_ge(gathered[s][u], 16 * UNIT * (k + 1))
                for c in range(NCHUNK):
                    if not first:
                        pe.wait_ge(rows_t_ready[c], t * NUNIT + u)
                    for n in range(UNIT):
                        last = nc.tensor.transpose(xp[c][:, n, :], rows[s][:, u * UNIT + n, c * P:(c + 1) * P],
                                                   ident[:, :])
                    last.then_inc(transposed[c], 1)

            def multiply(t, s, v, first=False):
                if v == 0:
                    for c in range(NCHUNK):
                        pe.wait_ge(rows_t_ready[c], (t + 1) * NUNIT)
                if not first:
                    pe.wait_ge(prod_act, t * NGU + v - 1)
                    pe.wait_ge(prod_dve, t * NGU + v - 1)
                for g in range(GPU):
                    for c in range(NCHUNK):
                        x = rows_t[s][:, c, v * GPU + g, :, :].rearrange("p j n -> p (j n)")
                        last = nc.tensor.matmul(gp[v % 2][:, g, :], x, x, start=(c == 0), stop=(c == NCHUNK - 1))
                last.then_inc(multiplied, 1)

            def mlp(t, first=False):
                pe.wait_ge(feat_ready, t + 1)
                pe.wait_ge(dense_loaded, 16 * (t + 1))
                if not first:
                    pe.wait_ge(y_ready, t)
                for k in range(K1):
                    last = nc.tensor.transpose(mp[:, k, :], feat[:, LEAD + k * P:LEAD + (k + 1) * P], ident[:, :])
                last.then_inc(feat_transposed, 1)
                pe.wait_ge(feat_t_ready, t + 1)
                for m in range(M1):
                    for k in range(K1):
                        last = nc.tensor.matmul(lp[:, m, :], w1_sb[:, k, m * P:(m + 1) * P], feat_t[:, k, :],
                                                start=(k == 0), stop=(k == K1 - 1))
                last.then_inc(layer1_done, 1)
                pe.wait_ge(hid1_ready, t + 1)
                for m in range(M2):
                    for k in range(M1):
                        last = nc.tensor.matmul(mp[:, m, :], w2_sb[:, k, m * P:(m + 1) * P], hid1[:, k, :],
                                                start=(k == 0), stop=(k == M1 - 1))
                last.then_inc(layer2_done, 1)
                pe.wait_ge(hid2_ready, t + 1)
                for k in range(M2):
                    last = nc.tensor.matmul(mp[0:1, M2, :], w3_sb[:, k:k + 1], hid2[:, k, :],
                                            start=(k == 0), stop=(k == M2 - 1))
                last.then_inc(layer3_done, 1)

            def step(t, k, first=False):
                s, o = (1, 0) if k is not None and parity[0] else (0, 1)
                for u in range(NUNIT - 1):
                    transpose_unit(t, s, k, u)
                    if u < NGU:
                        multiply(t - 1, o, u, first=first and u < 2)
                mlp(t - 1, first=first)
                transpose_unit(t, s, k, NUNIT - 1)

            parity = [0]
            pe.wait_ge(w_loaded, 16 * NWEIGHT)
            for u in range(NUNIT):
                transpose_unit(0, 0, 0, u, first=(u == 0))
            parity[0] = 1
            step(1, 0, first=True)
            with pe.Fori(1, ntile // 2) as k:
                parity[0] = 0
                step(2 * k, k)
                parity[0] = 1
                step(2 * k + 1, k)
            for v in range(NGU):
                multiply(ntile - 1, 1, v)
            mlp(ntile - 1)

        @block.scalar
        def _(act):
            def take_rows_t(t, s, u):
                act.wait_ge(transposed[0], t * NUNIT + u + 1)
                nc.scalar.copy(
                    rows_t[s][:, 0, :, :, u * UNIT:(u + 1) * UNIT].rearrange("p g j n -> p n j g"),
                    xp[0][:, :, :].rearrange("p n (j g) -> p n j g", j=NQUAD)).then_inc(rows_t_ready[0], 1)

            def take_products(t, v, first=False):
                act.wait_ge(multiplied, t * NGU + v + 1)
                if v == 0 and not first:
                    act.wait_ge(feat_ready, t)
                for j in (0, 1):
                    q = slice(32 * j, 32 * j + 32)
                    last = nc.scalar.copy(prod[q, v * GPU:(v + 1) * GPU, :],
                                          gp[v % 2][q, :, j * NFIELD:(j + 1) * NFIELD])
                last.then_inc(prod_act, 1)

            def mlp(t, first=False):
                act.wait_ge(feat_transposed, t + 1)
                nc.scalar.copy(feat_t[:, :, :], mp[:, :, :]).then_inc(feat_t_ready, 1)
                act.wait_ge(layer1_done, t + 1)
                for m in range(M1):
                    last = nc.scalar.activation(hid1[:, m, :], lp[:, m, :], ACT.Relu, bias=b1_sb[:, m:m + 1])
                last.then_inc(hid1_ready, 1)
                act.wait_ge(layer2_done, t + 1)
                for m in range(M2):
                    last = nc.scalar.activation(hid2[:, m, :], mp[:, m, :], ACT.Relu, bias=b2_sb[:, m:m + 1])
                last.then_inc(hid2_ready, 1)
                act.wait_ge(layer3_done, t + 1)
                if not first:
                    act.wait_ge(y_stored, 16 * t)
                nc.scalar.copy(y_row[0:1, :], mp[0:1, M2, :]).then_inc(y_ready, 1)

            def step(t, s, first=False):
                for u in range(NUNIT - 1):
                    take_rows_t(t, s, u)
                    if u < NGU:
                        take_products(t - 1, u, first=first)
                mlp(t - 1, first=first)
                take_rows_t(t, s, NUNIT - 1)

            act.wait_ge(w_loaded, 16 * NWEIGHT)
            for u in range(NUNIT):
                take_rows_t(0, 0, u)
            step(1, 1, first=True)
            with act.Fori(1, ntile // 2) as k:
                step(2 * k, 0)
                step(2 * k + 1, 1)
            for v in range(NGU):
                take_products(ntile - 1, v)
            mlp(ntile - 1)

        @block.vector
        def _(dve):
            def take_rows_t(t, s, u):
                dve.wait_ge(transposed[1], t * NUNIT + u + 1)
                nc.vector.tensor_copy(
                    rows_t[s][:, 1, :, :, u * UNIT:(u + 1) * UNIT].rearrange("p g j n -> p n j g"),
                    xp[1][:, :, :].rearrange("p n (j g) -> p n j g", j=NQUAD)).then_inc(rows_t_ready[1], 1)

            def take_products(t, v, first=False):
                dve.wait_ge(multiplied, t * NGU + v + 1)
                if v == 0 and not first:
                    dve.wait_ge(feat_ready, t)
                for j in (2, 3):
                    q = slice(32 * j, 32 * j + 32)
                    last = nc.vector.tensor_copy(prod[q, v * GPU:(v + 1) * GPU, :],
                                                 gp[v % 2][q, :, j * NFIELD:(j + 1) * NFIELD])
                last.then_inc(prod_dve, 1)

            def turn_products(t, first=False):
                dve.wait_ge(prod_act, (t + 1) * NGU)
                dve.wait_ge(prod_dve, (t + 1) * NGU)
                if not first:
                    dve.wait_ge(feat_transposed, t)
                for n, i in enumerate(reversed(range(NFIELD - 1))):
                    at = LEAD + first_pair(i) - (i + 1)
                    if n:
                        dve.wait_ge(turned, t * (NFIELD - 2) + n)
                    done = nc.vector.transpose(feat[:, at:at + NFIELD], prod[:, :, i])
                    done.then_inc(turned if i else feat_ready, 1)

            def step(t, s, first=False):
                for u in range(NUNIT):
                    take_rows_t(t, s, u)
                    if u < NGU:
                        take_products(t - 1, u, first=first)
                    if u == NGU - 1:
                        turn_products(t - 1, first=first)

            for u in range(NUNIT):
                take_rows_t(0, 0, u)
            step(1, 1, first=True)
            with dve.Fori(1, ntile // 2) as k:
                step(2 * k, 0)
                step(2 * k + 1, 1)
            for v in range(NGU):
                take_products(ntile - 1, v)
            turn_products(ntile - 1)


def kernel(**inputs):
    import numpy as np
    import concourse.bacc as bacc
    from concourse.bass_utils import run_bass_kernel_spmd

    nc = bacc.Bacc("TRN2", target_bir_lowering=False, num_devices=1)
    arrays = {}

    def give(name, a):
        a = np.ascontiguousarray(a)
        arrays[name] = a
        return nc.dram_tensor(name, a.shape, mybir.dt.from_np(a.dtype), kind="ExternalInput").ap()

    dense = give("dense_ctx", inputs["dense_ctx"])
    ids = give("ids", inputs["ids"])
    tables = [give(f"tbl_{n}", inputs[f"tbl_{n}"]) for n in range(NFIELD)]
    w1, b1, w2, b2, w3 = (give(n, inputs[n]) for n in ("W_top1", "b_top1", "W_top2", "b_top2", "W_top3"))
    eye = give("eye", np.eye(P, dtype=np.float32))
    out = nc.dram_tensor("y", (ids.shape[0], 1), mybir.dt.float32, kind="ExternalOutput").ap()
    dlrm_tower(nc, dense, ids, tables, w1, b1, w2, b2, w3, eye, out)
    r = run_bass_kernel_spmd(nc, [arrays], core_ids=[0])
    return r.results[0]["y"]
```

```python
from contextlib import ExitStack

import concourse.bass as bass
from concourse import mybir

P = 128
NFIELD = 32
NDIM = 256
NCHUNK = NDIM // P
NDENSE = 16
UNIT = 4
NUNIT = NFIELD // UNIT
NQUAD = 4
NGROUP = P // NQUAD
GPU = 8
NGU = NGROUP // GPU
NPAIR = NFIELD * (NFIELD - 1) // 2
ACT_ROWS = range(1, 27, 3)
SLOTS = 2


def first_pair(i):
    return i * (NFIELD - 1) - i * (i - 1) // 2


def dlrm_tower(nc, dense, ids, tables, w1, b1, w2, b2, w3, eye, out):
    fp32 = mybir.dt.float32
    int32 = mybir.dt.int32
    uint32 = mybir.dt.uint32
    ALU = mybir.AluOpType
    ACT = mybir.ActivationFunctionType

    batch = ids.shape[0]
    ntile = batch // P
    nin, nhid1 = w1.shape
    nhid2 = w2.shape[1]
    K1, M1, M2 = nin // P, nhid1 // P, nhid2 // P
    assert nin == NPAIR + NDENSE and ntile % 2 == 0 and ntile >= 4

    ctx = ExitStack()
    with ctx:
        def sb(name, shape, dt=fp32):
            return ctx.enter_context(nc.sbuf_tensor(name, shape, dt))

        def pb(name, shape):
            return ctx.enter_context(nc.psum_tensor(name, shape, fp32))

        def sem(name):
            return ctx.enter_context(nc.semaphore(name))

        ids_sb = [sb(f"ids_sb{s}", [P, NFIELD], int32) for s in range(SLOTS)]
        rows = [sb(f"rows{s}", [P, NFIELD, NDIM]) for s in range(SLOTS)]
        rows_t = [sb(f"rows_t{s}", [P, NCHUNK, NGROUP, NQUAD, NFIELD]) for s in range(SLOTS)]
        prod = sb("prod", [P, NGROUP, NFIELD])
        prod_t = sb("prod_t", [P, NFIELD, NFIELD])
        feat = sb("feat", [P, nin])
        feat_t = sb("feat_t", [P, K1, P])
        hid1 = sb("hid1", [P, M1, P])
        hid2 = sb("hid2", [P, M2, P])
        y_row = sb("y_row", [1, P])
        w1_sb = sb("w1_sb", [P, K1, nhid1])
        w2_sb = sb("w2_sb", [P, M1, nhid2])
        w3_sb = sb("w3_sb", [P, M2])
        b1_sb = sb("b1_sb", [P, M1])
        b2_sb = sb("b2_sb", [P, M2])
        ident = sb("ident", [P, P])

        xp = [pb(f"xp{c}", [P, UNIT, P]) for c in range(NCHUNK)]
        gp = [pb(f"gp{k}", [P, GPU, P]) for k in range(2)]
        mp = pb("mp", [P, 4, P])
        lp = pb("lp", [P, M1, P])

        w_loaded = sem("w_loaded")
        ids_loaded = [sem(f"ids_loaded{s}") for s in range(SLOTS)]
        dense_loaded = sem("dense_loaded")
        gathered = [[sem(f"gathered{s}_{u}") for u in range(NUNIT)] for s in range(SLOTS)]
        transposed = [sem(f"transposed{c}") for c in range(NCHUNK)]
        rows_t_ready = [sem(f"rows_t_ready{c}") for c in range(NCHUNK)]
        multiplied = sem("multiplied")
        prod_act = sem("prod_act")
        prod_dve = sem("prod_dve")
        turned = sem("turned")
        feat_ready = sem("feat_ready")
        feat_ready_act = sem("feat_ready_act")
        feat_transposed = sem("feat_transposed")
        feat_t_ready = sem("feat_t_ready")
        layer1_done = sem("layer1_done")
        hid1_ready = sem("hid1_ready")
        layer2_done = sem("layer2_done")
        hid2_ready = sem("hid2_ready")
        layer3_done = sem("layer3_done")
        y_ready = sem("y_ready")
        y_stored = sem("y_stored")
        NWEIGHT = 6

        def pairs_of(i):
            return feat[:, first_pair(i):first_pair(i + 1)], prod_t[:, i, i + 1:]

        block = ctx.enter_context(nc.Block())

        @block.sync
        def _(sp):
            def load_ids(at, s):
                sp.dma_start(ids_sb[s][:, :], ids[bass.ds(at, P), :]).then_inc(ids_loaded[s], 16)

            def load_dense(at):
                sp.dma_start(feat[:, NPAIR:], dense[bass.ds(at, P), :]).then_inc(dense_loaded, 16)

            load_ids(0, 0)
            load_ids(P, 1)
            sp.dma_start(ident[:, :], eye).then_inc(w_loaded, 16)
            load_dense(0)
            sp.dma_start(w1_sb[:, :, :], w1.rearrange("(k p) n -> p k n", p=P)).then_inc(w_loaded, 16)
            sp.dma_start(w2_sb[:, :, :], w2.rearrange("(k p) n -> p k n", p=P)).then_inc(w_loaded, 16)
            sp.dma_start(w3_sb[:, :], w3.rearrange("(k p) o -> p (k o)", p=P),
                         allow_slow_non_contiguous=True).then_inc(w_loaded, 16)
            sp.dma_start(b1_sb[:, :], b1.rearrange("(k p) -> p k", p=P),
                         allow_slow_non_contiguous=True).then_inc(w_loaded, 16)
            sp.dma_start(b2_sb[:, :], b2.rearrange("(k p) -> p k", p=P),
                         allow_slow_non_contiguous=True).then_inc(w_loaded, 16)

            def step(k, s, first=False):
                t = 2 * k + s
                here, dense_at, landed = (
                    x if first else sp.snap(x) for x in (t * P, (t - 2) * P, 16 * UNIT * k))
                for u in range(NUNIT):
                    sp.wait_ge(gathered[s][u], landed)
                load_ids(here, s)
                if not first or s == 1:
                    sp.wait_ge(feat_transposed, t - 2)
                    load_dense(dense_at)

            step(1, 0, first=True)
            step(1, 1, first=True)
            with sp.Fori(2, ntile // 2) as k:
                step(k, 0)
                step(k, 1)
            for t in (ntile - 2, ntile - 1):
                sp.wait_ge(feat_transposed, t)
                load_dense(t * P)
            sp.wait_ge(y_stored, 16 * ntile)

        @block.gpsimd
        def _(pool):
            def gather(s, k, first=False):
                pool.wait_ge(ids_loaded[s], 16 * (k + 1))
                for u in range(NUNIT):
                    if not first:
                        pool.wait_ge(transposed[NCHUNK - 1], units_used)
                        pool.reg_add(units_used, units_used, 1)
                    for n in range(u * UNIT, (u + 1) * UNIT):
                        pool.indirect_dma_start(
                            out=rows[s][:, n, :], out_offset=None, in_=tables[n][:, :],
                            in_offset=bass.IndirectOffsetOnAxis(ap=ids_sb[s][:, n:n + 1].bitcast(uint32), axis=0),
                        ).then_inc(gathered[s][u], 16)

            gather(0, 0, first=True)
            gather(1, 0, first=True)
            units_used = pool.alloc_register("units_used")
            pool.reg_mov(units_used, 1)
            with pool.Fori(1, ntile // 2) as k:
                gather(0, k)
                gather(1, k)

        @block.tensor
        def _(pe):
            def transpose_unit(t, s, k, u, first=False):
                pe.wait_ge(gathered[s][u], 16 * UNIT * (k + 1))
                for c in range(NCHUNK):
                    if not first:
                        pe.wait_ge(rows_t_ready[c], t * NUNIT + u)
                    for n in range(UNIT):
                        last = nc.tensor.transpose(xp[c][:, n, :], rows[s][:, u * UNIT + n, c * P:(c + 1) * P],
                                                   ident[:, :])
                    last.then_inc(transposed[c], 1)

            def multiply(t, s, v, first=False):
                if v == 0:
                    for c in range(NCHUNK):
                        pe.wait_ge(rows_t_ready[c], (t + 1) * NUNIT)
                if not first:
                    pe.wait_ge(prod_act, t * NGU + v - 1)
                    pe.wait_ge(prod_dve, t * NGU + v - 1)
                for g in range(GPU):
                    for c in range(NCHUNK):
                        x = rows_t[s][:, c, v * GPU + g, :, :].rearrange("p j n -> p (j n)")
                        last = nc.tensor.matmul(gp[v % 2][:, g, :], x, x, start=(c == 0), stop=(c == NCHUNK - 1))
                last.then_inc(multiplied, 1)

            def transpose_features(t, first=False, last_tile=False):
                pe.wait_ge(feat_ready, t + 1)
                if last_tile:
                    pe.wait_ge(feat_ready_act, 1)
                pe.wait_ge(dense_loaded, 16 * (t + 1))
                if not first:
                    pe.wait_ge(y_ready, t)
                for k in range(K1):
                    last = nc.tensor.transpose(mp[:, k, :], feat[:, k * P:(k + 1) * P], ident[:, :])
                last.then_inc(feat_transposed, 1)

            def layer1(t):
                pe.wait_ge(feat_t_ready, t + 1)
                for m in range(M1):
                    for k in range(K1):
                        last = nc.tensor.matmul(lp[:, m, :], w1_sb[:, k, m * P:(m + 1) * P], feat_t[:, k, :],
                                                start=(k == 0), stop=(k == K1 - 1))
                last.then_inc(layer1_done, 1)

            def layer2(t):
                pe.wait_ge(hid1_ready, t + 1)
                for m in range(M2):
                    for k in range(M1):
                        last = nc.tensor.matmul(mp[:, m, :], w2_sb[:, k, m * P:(m + 1) * P], hid1[:, k, :],
                                                start=(k == 0), stop=(k == M1 - 1))
                last.then_inc(layer2_done, 1)

            def layer3(t):
                pe.wait_ge(hid2_ready, t + 1)
                for k in range(M2):
                    last = nc.tensor.matmul(mp[0:1, M2, :], w3_sb[:, k:k + 1], hid2[:, k, :],
                                            start=(k == 0), stop=(k == M2 - 1))
                last.then_inc(layer3_done, 1)

            def step(k, s, first=False, second=False, final=False):
                t = 2 * k + s
                mlp = not first
                for u in range(NUNIT):
                    transpose_unit(t, s, k, u)
                    if u == 0 and mlp:
                        transpose_features(t - 2, first=second)
                    if u == 1 and mlp:
                        layer1(t - 2)
                    if u == 2 and mlp:
                        layer2(t - 2)
                    if u == 3 and mlp:
                        layer3(t - 2)
                    if u < NGU:
                        multiply(t - 1, 1 - s, u, first=first and u < 2)
                    if final and u == NUNIT - 2:
                        transpose_features(t - 1)
                        layer1(t - 1)
                if final:
                    layer2(t - 1)
                    layer3(t - 1)

            pe.wait_ge(w_loaded, 16 * NWEIGHT)
            for u in range(NUNIT):
                transpose_unit(0, 0, 0, u, first=(u == 0))
            step(0, 1, first=True)
            step(1, 0, second=True)
            step(1, 1)
            with pe.Fori(2, ntile // 2 - 1) as k:
                step(k, 0)
                step(k, 1)
            step(ntile // 2 - 1, 0)
            step(ntile // 2 - 1, 1, final=True)
            for v in range(NGU):
                multiply(ntile - 1, 1, v)
            transpose_features(ntile - 1, last_tile=True)
            layer1(ntile - 1)
            layer2(ntile - 1)
            layer3(ntile - 1)

        @block.scalar
        def _(act):
            def take_rows_t(t, s, u):
                act.wait_ge(transposed[0], t * NUNIT + u + 1)
                nc.scalar.copy(
                    rows_t[s][:, 0, :, :, u * UNIT:(u + 1) * UNIT].rearrange("p g j n -> p n j g"),
                    xp[0][:, :, :].rearrange("p n (j g) -> p n j g", j=NQUAD)).then_inc(rows_t_ready[0], 1)

            def take_products(t, v, first=False):
                act.wait_ge(multiplied, t * NGU + v + 1)
                if v == 0 and not first:
                    act.wait_ge(turned, t)
                for j in (0, 1):
                    q = slice(32 * j, 32 * j + 32)
                    last = nc.scalar.copy(prod[q, v * GPU:(v + 1) * GPU, :],
                                          gp[v % 2][q, :, j * NFIELD:(j + 1) * NFIELD])
                last.then_inc(prod_act, 1)

            def take_features(t):
                act.wait_ge(feat_transposed, t + 1)
                nc.scalar.copy(feat_t[:, :, :], mp[:, :, :]).then_inc(feat_t_ready, 1)

            def take_layer1(t):
                act.wait_ge(layer1_done, t + 1)
                for m in range(M1):
                    last = nc.scalar.activation(hid1[:, m, :], lp[:, m, :], ACT.Relu, bias=b1_sb[:, m:m + 1])
                last.then_inc(hid1_ready, 1)

            def take_layer2(t):
                act.wait_ge(layer2_done, t + 1)
                for m in range(M2):
                    last = nc.scalar.activation(hid2[:, m, :], mp[:, m, :], ACT.Relu, bias=b2_sb[:, m:m + 1])
                last.then_inc(hid2_ready, 1)

            def take_layer3(t, first=False):
                act.wait_ge(layer3_done, t + 1)
                if not first:
                    act.wait_ge(y_stored, 16 * t)
                nc.scalar.copy(y_row[0:1, :], mp[0:1, M2, :]).then_inc(y_ready, 1)
                act.wait_ge(y_ready, t + 1)
                act.dma_start(out[bass.ds(t * P, P), :].rearrange("b o -> o b"), y_row[0:1, :]).then_inc(y_stored, 16)

            def step(t, s, first=False, second=False, final=False):
                mlp = not first
                for u in range(NUNIT):
                    take_rows_t(t, s, u)
                    if u == 0 and mlp:
                        take_features(t - 2)
                    if u == 1 and mlp:
                        take_layer1(t - 2)
                    if u == 2 and mlp:
                        take_layer2(t - 2)
                    if u == 3 and mlp:
                        take_layer3(t - 2, first=second)
                    if u < NGU:
                        take_products(t - 1, u, first=first)
                    if final and u == NUNIT - 2:
                        take_features(t - 1)
                        take_layer1(t - 1)
                if final:
                    take_layer2(t - 1)
                    take_layer3(t - 1)

            act.wait_ge(w_loaded, 16 * NWEIGHT)
            for u in range(NUNIT):
                take_rows_t(0, 0, u)
            step(1, 1, first=True)
            step(2, 0, second=True)
            step(3, 1)
            with act.Fori(2, ntile // 2 - 1) as k:
                step(2 * k, 0)
                step(2 * k + 1, 1)
            step(ntile - 2, 0)
            step(ntile - 1, 1, final=True)
            for v in range(NGU):
                take_products(ntile - 1, v)
            act.wait_ge(turned, ntile)
            for i in ACT_ROWS:
                last = nc.scalar.copy(*pairs_of(i))
            last.then_inc(feat_ready_act, 1)
            take_features(ntile - 1)
            take_layer1(ntile - 1)
            take_layer2(ntile - 1)
            take_layer3(ntile - 1)

        @block.vector
        def _(dve):
            def take_rows_t(t, s, u):
                dve.wait_ge(transposed[1], t * NUNIT + u + 1)
                nc.vector.tensor_copy(
                    rows_t[s][:, 1, :, :, u * UNIT:(u + 1) * UNIT].rearrange("p g j n -> p n j g"),
                    xp[1][:, :, :].rearrange("p n (j g) -> p n j g", j=NQUAD)).then_inc(rows_t_ready[1], 1)

            def take_products(t, v, first=False):
                dve.wait_ge(multiplied, t * NGU + v + 1)
                if v == 0 and not first:
                    dve.wait_ge(turned, t)
                for j in (2, 3):
                    q = slice(32 * j, 32 * j + 32)
                    last = nc.vector.tensor_copy(prod[q, v * GPU:(v + 1) * GPU, :],
                                                 gp[v % 2][q, :, j * NFIELD:(j + 1) * NFIELD])
                last.then_inc(prod_dve, 1)

            def turn_products(t):
                dve.wait_ge(prod_act, (t + 1) * NGU)
                dve.wait_ge(prod_dve, (t + 1) * NGU)
                nc.vector.transpose(prod_t[:, :, :],
                                    prod[:, :, :].rearrange("p g i -> p i g")).then_inc(turned, 1)

            def order_pairs(t, fields, first=False):
                if fields[0] == 0:
                    dve.wait_ge(turned, t + 1)
                    if not first:
                        dve.wait_ge(feat_transposed, t)
                for i in fields:
                    last = nc.vector.tensor_copy(*pairs_of(i))
                if fields[-1] >= NFIELD - 3:
                    last.then_inc(feat_ready, 1)

            def step(t, s, first=False):
                for u in range(NUNIT):
                    take_rows_t(t, s, u)
                    if u < NGU:
                        take_products(t - 1, u, first=first)
                    if u == NGU - 1:
                        turn_products(t - 1)
                        order_pairs(t - 1, range(0, 10), first=first)
                    if u == NGU:
                        order_pairs(t - 1, range(10, NFIELD - 1), first=first)

            for u in range(NUNIT):
                take_rows_t(0, 0, u)
            step(1, 1, first=True)
            with dve.Fori(1, ntile // 2) as k:
                step(2 * k, 0)
                step(2 * k + 1, 1)
            for v in range(NGU):
                take_products(ntile - 1, v)
            turn_products(ntile - 1)
            order_pairs(ntile - 1, [i for i in range(NFIELD - 1) if i not in ACT_ROWS])


def kernel(**inputs):
    import numpy as np
    import concourse.bacc as bacc
    from concourse.bass_utils import run_bass_kernel_spmd

    nc = bacc.Bacc("TRN2", target_bir_lowering=False, num_devices=1)
    arrays = {}

    def give(name, a):
        a = np.ascontiguousarray(a)
        arrays[name] = a
        return nc.dram_tensor(name, a.shape, mybir.dt.from_np(a.dtype), kind="ExternalInput").ap()

    dense = give("dense_ctx", inputs["dense_ctx"])
    ids = give("ids", inputs["ids"])
    tables = [give(f"tbl_{n}", inputs[f"tbl_{n}"]) for n in range(NFIELD)]
    w1, b1, w2, b2, w3 = (give(n, inputs[n]) for n in ("W_top1", "b_top1", "W_top2", "b_top2", "W_top3"))
    eye = give("eye", np.eye(P, dtype=np.float32))
    out = nc.dram_tensor("y", (ids.shape[0], 1), mybir.dt.float32, kind="ExternalOutput").ap()
    dlrm_tower(nc, dense, ids, tables, w1, b1, w2, b2, w3, eye, out)
    r = run_bass_kernel_spmd(nc, [arrays], core_ids=[0])
    return r.results[0]["y"]
```

```python
from contextlib import ExitStack

import concourse.bass as bass
from concourse import mybir

P = 128
NFIELD = 32
NDIM = 256
NCHUNK = NDIM // P
NDENSE = 16
UNIT = 4
NUNIT = NFIELD // UNIT
NQUAD = 4
NGROUP = P // NQUAD
GPU = 8
NGU = NGROUP // GPU
NPAIR = NFIELD * (NFIELD - 1) // 2
DVE_PAIRS = [i for i in range(NFIELD - 1) if i % 3]
ORDER_PARTS = (range(0, 10), range(10, 20), range(20, NFIELD - 1))
PRODUCTS_AT = (0, 1, 2, 3)
SLOTS = 2


def first_pair(i):
    return i * (NFIELD - 1) - i * (i - 1) // 2


def dlrm_tower(nc, dense, ids, tables, w1, b1, w2, b2, w3, eye, out):
    fp32 = mybir.dt.float32
    int32 = mybir.dt.int32
    uint32 = mybir.dt.uint32
    ACT = mybir.ActivationFunctionType

    batch = ids.shape[0]
    ntile = batch // P
    nin, nhid1 = w1.shape
    nhid2 = w2.shape[1]
    K1, M1, M2 = nin // P, nhid1 // P, nhid2 // P
    assert nin == NPAIR + NDENSE and ntile % 2 == 0 and ntile >= 4

    ctx = ExitStack()
    with ctx:
        def sb(name, shape, dt=fp32):
            return ctx.enter_context(nc.sbuf_tensor(name, shape, dt))

        def pb(name, shape):
            return ctx.enter_context(nc.psum_tensor(name, shape, fp32))

        def sem(name):
            return ctx.enter_context(nc.semaphore(name))

        ids_sb = [sb(f"ids_sb{s}", [P, NFIELD], int32) for s in range(SLOTS)]
        rows = [sb(f"rows{s}", [P, NFIELD, NDIM]) for s in range(SLOTS)]
        rows_t = [sb(f"rows_t{s}", [P, NCHUNK, NGROUP, NQUAD, NFIELD]) for s in range(SLOTS)]
        prod = sb("prod", [P, NGROUP, NFIELD])
        prod_t = sb("prod_t", [P, NFIELD, NFIELD])
        feat = sb("feat", [P, nin])
        feat_t = sb("feat_t", [P, K1, P])
        hid1 = sb("hid1", [P, M1, P])
        hid2 = sb("hid2", [P, M2, P])
        y_row = sb("y_row", [1, SLOTS, P])
        w1_sb = sb("w1_sb", [P, K1, nhid1])
        w2_sb = sb("w2_sb", [P, M1, nhid2])
        w3_sb = sb("w3_sb", [P, M2])
        b1_sb = sb("b1_sb", [P, M1])
        b2_sb = sb("b2_sb", [P, M2])
        ident = sb("ident", [P, P])

        xp = [pb(f"xp{c}", [P, UNIT, P]) for c in range(NCHUNK)]
        gp = [pb(f"gp{k}", [P, GPU, P]) for k in range(2)]
        mp = pb("mp", [P, 4, P])
        lp = pb("lp", [P, M1, P])

        w_loaded = sem("w_loaded")
        ids_loaded = [sem(f"ids_loaded{s}") for s in range(SLOTS)]
        dense_loaded = sem("dense_loaded")
        gathered = [[sem(f"gathered{s}_{u}") for u in range(NUNIT)] for s in range(SLOTS)]
        transposed = [sem(f"transposed{c}") for c in range(NCHUNK)]
        rows_t_ready = [sem(f"rows_t_ready{c}") for c in range(NCHUNK)]
        multiplied = sem("multiplied")
        prod_act = sem("prod_act")
        prod_dve = sem("prod_dve")
        turned = sem("turned")
        feat_ready = sem("feat_ready")
        feat_ready_dve = sem("feat_ready_dve")
        feat_transposed = sem("feat_transposed")
        feat_t_ready = sem("feat_t_ready")
        layer1_done = sem("layer1_done")
        hid1_ready = sem("hid1_ready")
        layer2_done = sem("layer2_done")
        hid2_ready = sem("hid2_ready")
        layer3_done = sem("layer3_done")
        y_ready = sem("y_ready")
        y_stored = [sem(f"y_stored{s}") for s in range(SLOTS)]
        NWEIGHT = 6

        def pairs_of(i):
            return feat[:, first_pair(i):first_pair(i + 1)], prod_t[:, i, i + 1:]

        mlp_psum = (mp[:, :, :], lp[:, :, :], mp[:, :, :])
        last_psum = (gp[0][:, 0:K1, :], gp[0][:, GPU // 2:GPU // 2 + M1, :], gp[1][:, 0:M2 + 1, :])

        def loop(engine, start, end):
            return nc.Fori(start, end, engines=(engine.engine,), hint_back_edge=True)

        block = ctx.enter_context(nc.Block())

        @block.sync
        def _(sp):
            def load_ids(at, s):
                sp.dma_start(ids_sb[s][:, :], ids[bass.ds(at, P), :]).then_inc(ids_loaded[s], 16)

            def load_dense(at):
                sp.dma_start(feat[:, NPAIR:], dense[bass.ds(at, P), :]).then_inc(dense_loaded, 16)

            load_ids(0, 0)
            load_ids(P, 1)
            sp.dma_start(ident[:, :], eye).then_inc(w_loaded, 16)
            load_dense(0)
            sp.dma_start(w1_sb[:, :, :], w1.rearrange("(k p) n -> p k n", p=P)).then_inc(w_loaded, 16)
            sp.dma_start(w2_sb[:, :, :], w2.rearrange("(k p) n -> p k n", p=P)).then_inc(w_loaded, 16)
            sp.dma_start(w3_sb[:, :], w3.rearrange("(k p) o -> p (k o)", p=P),
                         allow_slow_non_contiguous=True).then_inc(w_loaded, 16)
            sp.dma_start(b1_sb[:, :], b1.rearrange("(k p) -> p k", p=P),
                         allow_slow_non_contiguous=True).then_inc(w_loaded, 16)
            sp.dma_start(b2_sb[:, :], b2.rearrange("(k p) -> p k", p=P),
                         allow_slow_non_contiguous=True).then_inc(w_loaded, 16)

            def step(k, s, first=False):
                t = 2 * k + s
                here, dense_at, landed = (
                    x if first else sp.snap(x) for x in (t * P, (t - 2) * P, 16 * UNIT * k))
                for u in range(NUNIT):
                    sp.wait_ge(gathered[s][u], landed)
                load_ids(here, s)
                if not first or s == 1:
                    sp.wait_ge(feat_transposed, t - 2)
                    load_dense(dense_at)

            step(1, 0, first=True)
            step(1, 1, first=True)
            with loop(sp, 2, ntile // 2) as k:
                step(k, 0)
                step(k, 1)
            for t in (ntile - 2, ntile - 1):
                sp.wait_ge(feat_transposed, t)
                load_dense(t * P)
            for s in range(SLOTS):
                sp.wait_ge(y_stored[s], 16 * ntile // SLOTS)

        @block.gpsimd
        def _(pool):
            def gather(s, k, first=False):
                pool.wait_ge(ids_loaded[s], 16 * (k + 1))
                for u in range(NUNIT):
                    if not first:
                        pool.wait_ge(transposed[NCHUNK - 1], units_used)
                        pool.reg_add(units_used, units_used, 1)
                    for n in range(u * UNIT, (u + 1) * UNIT):
                        pool.indirect_dma_start(
                            out=rows[s][:, n, :], out_offset=None, in_=tables[n][:, :],
                            in_offset=bass.IndirectOffsetOnAxis(ap=ids_sb[s][:, n:n + 1].bitcast(uint32), axis=0),
                        ).then_inc(gathered[s][u], 16)

            gather(0, 0, first=True)
            gather(1, 0, first=True)
            units_used = pool.alloc_register("units_used")
            pool.reg_mov(units_used, 1)
            with loop(pool, 1, ntile // 2) as k:
                gather(0, k)
                gather(1, k)

        @block.tensor
        def _(pe):
            def transpose_unit(t, s, k, u, first=False):
                pe.wait_ge(gathered[s][u], 16 * UNIT * (k + 1))
                for c in range(NCHUNK):
                    if not first:
                        pe.wait_ge(rows_t_ready[c], t * NUNIT + u)
                    for n in range(UNIT):
                        last = nc.tensor.transpose(xp[c][:, n, :], rows[s][:, u * UNIT + n, c * P:(c + 1) * P],
                                                   ident[:, :])
                    last.then_inc(transposed[c], 1)

            def multiply(t, s, v, first=False):
                if v == 0:
                    for c in range(NCHUNK):
                        pe.wait_ge(rows_t_ready[c], (t + 1) * NUNIT)
                if not first:
                    pe.wait_ge(prod_act, t * NGU + v - 1)
                    pe.wait_ge(prod_dve, t * NGU + v - 1)
                for g in range(GPU):
                    for c in range(NCHUNK):
                        x = rows_t[s][:, c, v * GPU + g, :, :].rearrange("p j n -> p (j n)")
                        last = nc.tensor.matmul(gp[v % 2][:, g, :], x, x, start=(c == 0), stop=(c == NCHUNK - 1))
                last.then_inc(multiplied, 1)

            def transpose_features(t, psum=mlp_psum, first=False):
                pe.wait_ge(feat_ready, t + 1)
                if psum is last_psum:
                    pe.wait_ge(feat_ready_dve, 1)
                elif not first:
                    pe.wait_ge(y_ready, t)
                pe.wait_ge(dense_loaded, 16 * (t + 1))
                for k in range(K1):
                    last = nc.tensor.transpose(psum[0][:, k, :], feat[:, k * P:(k + 1) * P], ident[:, :])
                last.then_inc(feat_transposed, 1)

            def layer1(t, psum=mlp_psum):
                pe.wait_ge(feat_t_ready, t + 1)
                for m in range(M1):
                    for k in range(K1):
                        last = nc.tensor.matmul(psum[1][:, m, :], w1_sb[:, k, m * P:(m + 1) * P], feat_t[:, k, :],
                                                start=(k == 0), stop=(k == K1 - 1))
                last.then_inc(layer1_done, 1)

            def layer2(t, psum=mlp_psum):
                pe.wait_ge(hid1_ready, t + 1)
                for m in range(M2):
                    for k in range(M1):
                        last = nc.tensor.matmul(psum[2][:, m, :], w2_sb[:, k, m * P:(m + 1) * P], hid1[:, k, :],
                                                start=(k == 0), stop=(k == M1 - 1))
                last.then_inc(layer2_done, 1)

            def layer3(t, psum=mlp_psum):
                pe.wait_ge(hid2_ready, t + 1)
                for k in range(M2):
                    last = nc.tensor.matmul(psum[2][0:1, M2, :], w3_sb[:, k:k + 1], hid2[:, k, :],
                                            start=(k == 0), stop=(k == M2 - 1))
                last.then_inc(layer3_done, 1)

            def step(t, s, k, first=False, second=False):
                for u in range(NUNIT):
                    transpose_unit(t, s, k, u)
                    if u == 1 and not first:
                        transpose_features(t - 2, first=second)
                    if u == 2 and not first:
                        layer1(t - 2)
                    if u == 3 and not first:
                        layer2(t - 2)
                    if u == 4 and not first:
                        layer3(t - 2)
                    if u in PRODUCTS_AT:
                        v = PRODUCTS_AT.index(u)
                        multiply(t - 1, 1 - s, v, first=first and v < 2)

            pe.wait_ge(w_loaded, 16 * NWEIGHT)
            for u in range(NUNIT):
                transpose_unit(0, 0, 0, u, first=(u == 0))
            step(1, 1, 0, first=True)
            step(2, 0, 1, second=True)
            with loop(pe, 1, ntile // 2 - 1) as k:
                step(2 * k + 1, 1, k)
                step(2 * k + 2, 0, k + 1)
            step(ntile - 1, 1, ntile // 2 - 1)
            n, o = ntile - 1, ntile - 2
            multiply(n, 1, 0)
            transpose_features(o)
            for v in range(1, NGU):
                multiply(n, 1, v)
            layer1(o)
            transpose_features(n, last_psum)
            layer2(o)
            layer1(n, last_psum)
            layer3(o)
            layer2(n, last_psum)
            layer3(n, last_psum)

        @block.scalar
        def _(act):
            def take_rows_t(t, s, u):
                act.wait_ge(transposed[0], t * NUNIT + u + 1)
                nc.scalar.copy(
                    rows_t[s][:, 0, :, :, u * UNIT:(u + 1) * UNIT].rearrange("p g j n -> p n j g"),
                    xp[0][:, :, :].rearrange("p n (j g) -> p n j g", j=NQUAD)).then_inc(rows_t_ready[0], 1)

            def take_products(t, v, first=False):
                act.wait_ge(multiplied, t * NGU + v + 1)
                if v == 0 and not first:
                    act.wait_ge(turned, t)
                for j in (0, 1):
                    q = slice(32 * j, 32 * j + 32)
                    last = nc.scalar.copy(prod[q, v * GPU:(v + 1) * GPU, :],
                                          gp[v % 2][q, :, j * NFIELD:(j + 1) * NFIELD])
                last.then_inc(prod_act, 1)

            def order_pairs(t, fields, wait=True, first=False, done=True):
                if wait:
                    act.wait_ge(turned, t + 1)
                if wait and not first:
                    act.wait_ge(feat_transposed, t)
                for i in fields:
                    last = nc.scalar.copy(*pairs_of(i))
                if done:
                    last.then_inc(feat_ready, 1)

            def take_features(t, psum=mlp_psum):
                act.wait_ge(feat_transposed, t + 1)
                nc.scalar.copy(feat_t[:, :, :], psum[0]).then_inc(feat_t_ready, 1)

            def take_layer1(t, psum=mlp_psum):
                act.wait_ge(layer1_done, t + 1)
                for m in range(M1):
                    last = nc.scalar.activation(hid1[:, m, :], psum[1][:, m, :], ACT.Relu, bias=b1_sb[:, m:m + 1])
                last.then_inc(hid1_ready, 1)

            def take_layer2(t, psum=mlp_psum):
                act.wait_ge(layer2_done, t + 1)
                for m in range(M2):
                    last = nc.scalar.activation(hid2[:, m, :], psum[2][:, m, :], ACT.Relu, bias=b2_sb[:, m:m + 1])
                last.then_inc(hid2_ready, 1)

            def take_layer3(t, s, k, psum=mlp_psum, first=False):
                act.wait_ge(layer3_done, t + 1)
                if not first:
                    act.wait_ge(y_stored[s], 16 * k)
                nc.scalar.copy(y_row[0:1, s, :], psum[2][0:1, M2, :]).then_inc(y_ready, 1)
                act.wait_ge(y_ready, t + 1)
                act.dma_start(out[bass.ds(t * P, P), :].rearrange("b o -> o b"),
                              y_row[0:1, s, :]).then_inc(y_stored[s], 16)

            def step(t, s, k, first=False, early=False):
                for u in range(NUNIT):
                    take_rows_t(t, s, u)
                    if u == 1 and not first:
                        take_features(t - 2)
                    if u == 2 and not first:
                        take_layer1(t - 2)
                    if u == 3 and not first:
                        take_layer2(t - 2)
                    if u == 4 and not first:
                        take_layer3(t - 2, s, k - 1, first=early)
                    if u in PRODUCTS_AT:
                        take_products(t - 1, PRODUCTS_AT.index(u), first=first)
                    if u >= NUNIT - len(ORDER_PARTS):
                        part = u - (NUNIT - len(ORDER_PARTS))
                        order_pairs(t - 1, ORDER_PARTS[part], wait=(part == 0), first=first,
                                    done=(part == len(ORDER_PARTS) - 1))

            act.wait_ge(w_loaded, 16 * NWEIGHT)
            for u in range(NUNIT):
                take_rows_t(0, 0, u)
            step(1, 1, 0, first=True)
            step(2, 0, 1, early=True)
            step(3, 1, 1, early=True)
            step(4, 0, 2)
            with loop(act, 2, ntile // 2 - 1) as k:
                step(2 * k + 1, 1, k)
                step(2 * k + 2, 0, k + 1)
            step(ntile - 1, 1, ntile // 2 - 1)
            n, o, k = ntile - 1, ntile - 2, ntile // 2 - 1
            take_products(n, 0)
            take_features(o)
            for v in range(1, NGU):
                take_products(n, v)
            order_pairs(n, [i for i in range(NFIELD - 1) if i not in DVE_PAIRS])
            take_layer1(o)
            take_features(n, last_psum)
            take_layer2(o)
            take_layer1(n, last_psum)
            take_layer3(o, 0, k)
            take_layer2(n, last_psum)
            take_layer3(n, 1, k, last_psum)

        @block.vector
        def _(dve):
            def take_rows_t(t, s, u):
                dve.wait_ge(transposed[1], t * NUNIT + u + 1)
                nc.vector.tensor_copy(
                    rows_t[s][:, 1, :, :, u * UNIT:(u + 1) * UNIT].rearrange("p g j n -> p n j g"),
                    xp[1][:, :, :].rearrange("p n (j g) -> p n j g", j=NQUAD)).then_inc(rows_t_ready[1], 1)

            def take_products(t, v, first=False):
                dve.wait_ge(multiplied, t * NGU + v + 1)
                if v == 0 and not first:
                    dve.wait_ge(turned, t)
                for j in (2, 3):
                    q = slice(32 * j, 32 * j + 32)
                    last = nc.vector.tensor_copy(prod[q, v * GPU:(v + 1) * GPU, :],
                                                 gp[v % 2][q, :, j * NFIELD:(j + 1) * NFIELD])
                last.then_inc(prod_dve, 1)

            def turn_products(t, first=False):
                dve.wait_ge(prod_act, (t + 1) * NGU)
                dve.wait_ge(prod_dve, (t + 1) * NGU)
                if not first:
                    dve.wait_ge(feat_ready, t)
                nc.vector.transpose(prod_t[:, :, :],
                                    prod[:, :, :].rearrange("p g i -> p i g")).then_inc(turned, 1)

            def step(t, s, first=False):
                for u in range(NUNIT):
                    take_rows_t(t, s, u)
                    if u in PRODUCTS_AT:
                        take_products(t - 1, PRODUCTS_AT.index(u), first=first)
                    if u == PRODUCTS_AT[-1]:
                        turn_products(t - 1, first=first)

            for u in range(NUNIT):
                take_rows_t(0, 0, u)
            step(1, 1, first=True)
            with loop(dve, 1, ntile // 2) as k:
                step(2 * k, 0)
                step(2 * k + 1, 1)
            for v in range(NGU):
                take_products(ntile - 1, v)
            turn_products(ntile - 1)
            dve.wait_ge(turned, ntile)
            dve.wait_ge(feat_transposed, ntile - 1)
            for i in DVE_PAIRS:
                last = nc.vector.tensor_copy(*pairs_of(i))
            last.then_inc(feat_ready_dve, 1)


def kernel(**inputs):
    import numpy as np
    import concourse.bacc as bacc
    from concourse.bass_utils import run_bass_kernel_spmd

    nc = bacc.Bacc("TRN2", target_bir_lowering=False, num_devices=1)
    arrays = {}

    def give(name, a):
        a = np.ascontiguousarray(a)
        arrays[name] = a
        return nc.dram_tensor(name, a.shape, mybir.dt.from_np(a.dtype), kind="ExternalInput").ap()

    dense = give("dense_ctx", inputs["dense_ctx"])
    ids = give("ids", inputs["ids"])
    tables = [give(f"tbl_{n}", inputs[f"tbl_{n}"]) for n in range(NFIELD)]
    w1, b1, w2, b2, w3 = (give(n, inputs[n]) for n in ("W_top1", "b_top1", "W_top2", "b_top2", "W_top3"))
    eye = give("eye", np.eye(P, dtype=np.float32))
    out = nc.dram_tensor("y", (ids.shape[0], 1), mybir.dt.float32, kind="ExternalOutput").ap()
    dlrm_tower(nc, dense, ids, tables, w1, b1, w2, b2, w3, eye, out)
    r = run_bass_kernel_spmd(nc, [arrays], core_ids=[0])
    return r.results[0]["y"]
```
